# Optimizing a Trainium2 kernel written in Bass

```python
import numpy as np
import jax
import jax.numpy as jnp

def _softmax(x, axis=-1):
    return jax.nn.softmax(x, axis=axis)

def _gelu(x):
    return jax.nn.gelu(x, approximate=True)

def _silu(x):
    return jax.nn.silu(x)

def _sigmoid(x):
    return jax.nn.sigmoid(x)

def _layernorm(x, axis=-1, eps=1e-05):
    m = jnp.mean(x, axis=axis, keepdims=True)
    v = jnp.var(x, axis=axis, keepdims=True)
    return (x - m) / jnp.sqrt(v + eps)

def _scatter_add(tgt, idx, src, axis=0):
    return tgt.at[idx].add(src)

def _segment_sum(src, seg, n):
    return jax.ops.segment_sum(src, seg, n)
kernel_name = 'mk_rec_standalone_d1_rec_r8_511c1a'

def setup_inputs(seed: int=0):
    np.random.seed(seed)
    _w = jnp.asarray

    def _rec_inputs():
        import jax
        import jax.numpy as jnp
        _rk = jax.random.key(seed)
        r_x_dense = -0.00338568 + 1.0005 * jax.random.normal(jax.random.fold_in(_rk, 1), (512, 13), jnp.float32)
        r_x_sparse = jnp.stack([jax.random.randint(jax.random.fold_in(jax.random.fold_in(_rk, 2), 0), (512,), 6, 49999, jnp.int32), jax.random.randint(jax.random.fold_in(jax.random.fold_in(_rk, 2), 1), (512,), 4, 49989, jnp.int32), jax.random.randint(jax.random.fold_in(jax.random.fold_in(_rk, 2), 2), (512,), 0, 49999, jnp.int32), jax.random.randint(jax.random.fold_in(jax.random.fold_in(_rk, 2), 3), (512,), 0, 49991, jnp.int32), jax.random.randint(jax.random.fold_in(jax.random.fold_in(_rk, 2), 4), (512,), 1, 49996, jnp.int32), jax.random.randint(jax.random.fold_in(jax.random.fold_in(_rk, 2), 5), (512,), 1, 6250, jnp.int32), jax.random.randint(jax.random.fold_in(jax.random.fold_in(_rk, 2), 6), (512,), 0, 49994, jnp.int32), jax.random.randint(jax.random.fold_in(jax.random.fold_in(_rk, 2), 7), (512,), 6, 49999, jnp.int32), jax.random.randint(jax.random.fold_in(jax.random.fold_in(_rk, 2), 8), (512,), 0, 6250, jnp.int32), jax.random.randint(jax.random.fold_in(jax.random.fold_in(_rk, 2), 9), (512,), 5, 49999, jnp.int32), jax.random.randint(jax.random.fold_in(jax.random.fold_in(_rk, 2), 10), (512,), 2, 49994, jnp.int32), jax.random.randint(jax.random.fold_in(jax.random.fold_in(_rk, 2), 11), (512,), 5, 49997, jnp.int32), jax.random.randint(jax.random.fold_in(jax.random.fold_in(_rk, 2), 12), (512,), 0, 49999, jnp.int32), jax.random.randint(jax.random.fold_in(jax.random.fold_in(_rk, 2), 13), (512,), 1, 49998, jnp.int32), jax.random.randint(jax.random.fold_in(jax.random.fold_in(_rk, 2), 14), (512,), 1, 49994, jnp.int32), jax.random.randint(jax.random.fold_in(jax.random.fold_in(_rk, 2), 15), (512,), 2, 6250, jnp.int32), jax.random.randint(jax.random.fold_in(jax.random.fold_in(_rk, 2), 16), (512,), 4, 49999, jnp.int32), jax.random.randint(jax.random.fold_in(jax.random.fold_in(_rk, 2), 17), (512,), 0, 6250, jnp.int32), jax.random.randint(jax.random.fold_in(jax.random.fold_in(_rk, 2), 18), (512,), 1, 49998, jnp.int32), jax.random.randint(jax.random.fold_in(jax.random.fold_in(_rk, 2), 19), (512,), 1, 49998, jnp.int32), jax.random.randint(jax.random.fold_in(jax.random.fold_in(_rk, 2), 20), (512,), 2, 49998, jnp.int32), jax.random.randint(jax.random.fold_in(jax.random.fold_in(_rk, 2), 21), (512,), 2, 49995, jnp.int32), jax.random.randint(jax.random.fold_in(jax.random.fold_in(_rk, 2), 22), (512,), 3, 49998, jnp.int32), jax.random.randint(jax.random.fold_in(jax.random.fold_in(_rk, 2), 23), (512,), 2, 49997, jnp.int32), jax.random.randint(jax.random.fold_in(jax.random.fold_in(_rk, 2), 24), (512,), 9, 6250, jnp.int32), jax.random.randint(jax.random.fold_in(jax.random.fold_in(_rk, 2), 25), (512,), 2, 49993, jnp.int32)], axis=1)
        return (r_x_dense, r_x_sparse)
    r_x_dense, r_x_sparse = _rec_inputs()

    def _L0_rec_setup():
        import jax, jax.numpy as jnp
        import numpy as np
        N_DENSE = 13
        N_FIELDS = 26
        VOCAB = 6250
        K = 64
        BATCH = 2048
        HID = N_FIELDS * (N_FIELDS - 1) // 2 + N_FIELDS * K + N_DENSE
        key = jax.random.key(seed)
        ks = jax.random.split(key, 7)
        x_dense = jax.random.normal(ks[0], (BATCH, N_DENSE), dtype=jnp.float32)
        x_sparse = jax.random.randint(ks[1], (BATCH, N_FIELDS), 0, VOCAB)
        lim_e = np.sqrt(6.0 / (VOCAB + K))
        emb_tables = jax.random.uniform(ks[2], (N_FIELDS, VOCAB, K), minval=-lim_e, maxval=lim_e, dtype=jnp.float32)
        lim1 = np.sqrt(1.0 / HID)
        w1 = jax.random.uniform(ks[3], (HID, HID), minval=-lim1, maxval=lim1, dtype=jnp.float32)
        b1 = jax.random.uniform(ks[4], (HID,), minval=-lim1, maxval=lim1, dtype=jnp.float32)
        w2 = jax.random.uniform(ks[5], (HID, 1), minval=-lim1, maxval=lim1, dtype=jnp.float32)
        b2 = jax.random.uniform(ks[6], (1,), minval=-lim1, maxval=lim1, dtype=jnp.float32)
        return {'x_dense': x_dense, 'x_sparse': x_sparse, 'emb_tables': emb_tables, 'w1': w1, 'b1': b1, 'w2': w2, 'b2': b2}
    _L0_rec_all = _L0_rec_setup()
    _L0_rec_in = {k: v for k, v in _L0_rec_all.items() if k in ('emb_tables', 'w1', 'b1', 'w2', 'b2')}
    del _L0_rec_all
    return {'r_x_dense': r_x_dense, 'r_x_sparse': r_x_sparse, 'L0_rec_emb_tables': _L0_rec_in['emb_tables'], 'L0_rec_w1': _L0_rec_in['w1'], 'L0_rec_b1': _L0_rec_in['b1'], 'L0_rec_w2': _L0_rec_in['w2'], 'L0_rec_b2': _L0_rec_in['b2']}

def reference(r_x_dense, r_x_sparse, L0_rec_emb_tables, L0_rec_w1, L0_rec_b1, L0_rec_w2, L0_rec_b2):
    import jax
    import jax.numpy as jnp

    def _L0_rec_ref(x_dense, x_sparse, emb_tables, w1, b1, w2, b2):
        import jax, jax.numpy as jnp
        import numpy as np
        N_DENSE = 13
        N_FIELDS = 26
        VOCAB = 6250
        K = 64
        BATCH = 2048
        HID = N_FIELDS * (N_FIELDS - 1) // 2 + N_FIELDS * K + N_DENSE
        B = x_dense.shape[0]
        field_idx = jnp.arange(N_FIELDS)
        sparse_embed = emb_tables[field_idx[None, :], x_sparse]
        z = sparse_embed.reshape(B, N_FIELDS * K)
        gram = jnp.einsum('bik,bjk->bij', sparse_embed, sparse_embed)
        iu, ju = jnp.triu_indices(N_FIELDS, k=1)
        inner = gram[:, iu, ju]
        dnn_in = jnp.concatenate([x_dense, z, inner], axis=-1)
        h = jax.nn.relu(dnn_in @ w1 + b1)
        out = jax.nn.sigmoid(h @ w2 + b2)
        return out
    y = _L0_rec_ref(r_x_dense, r_x_sparse, L0_rec_emb_tables, L0_rec_w1, L0_rec_b1, L0_rec_w2, L0_rec_b2)
    return y

_drawn_inputs = setup_inputs


def setup_inputs(seed=0):
    import zlib

    import numpy as np

    out = dict(_drawn_inputs(seed))
    spreads = {}
    factors = {'r_x_dense': 5.492,
     'L0_rec_emb_tables': 8.0,
     'L0_rec_w1': 6.258,
     'L0_rec_b1': 8.0,
     'L0_rec_w2': 7.857}
    for name, (base, spread) in spreads.items():
        noise = np.random.default_rng([zlib.crc32(name.encode()), seed]).standard_normal(out[name].shape)
        drawn = base * np.exp(spread * noise) if base else spread * noise
        out[name] = jnp.asarray(drawn.astype(out[name].dtype))
    for name, factor in factors.items():
        out[name] = (out[name] * factor).astype(out[name].dtype)
    return out
```

```python
from contextlib import ExitStack

import concourse.bass as bass
from concourse import mybir

ALU = mybir.AluOpType
ACT = mybir.ActivationFunctionType
AX = mybir.AxisListType
F32 = mybir.dt.float32
F32R = mybir.dt.float32r
I32 = mybir.dt.int32
U32 = mybir.dt.uint32

P = 128
BATCH, DENSE, FIELDS, VOCAB, K = 512, 13, 26, 6250, 64
PAIRS = FIELDS * (FIELDS - 1) // 2
HID = DENSE + FIELDS * K + PAIRS
BT = BATCH // P

ZT = FIELDS // 2
ROWS_G = FIELDS * FIELDS
HALF = FIELDS // 2
BLOCK_A = [9, 9, 7]
INNER = [n * HALF for n in BLOCK_A]
IT = len(BLOCK_A)
DENSE_AT = 96
NT = ZT + IT
KROWS = [P] * ZT + INNER[:-1] + [DENSE_AT + DENSE + 1]

CHUNKS = [[(0, 502), (502, 500)], [(1002, 500), (1502, 500)]]
HALF_AT = [0, 1002]
HALF_W = [1002, 1000]
HW = max(HALF_W)

RAW = 5
HL = 5
GROUPS = P // 4
PER_BANK = 4
ROUNDS = GROUPS // PER_BANK
AUX = 6
LEAD = 3
FETCH = 7

PIECES = ([(0, t, h) for t in range(NT) for h in (0, 1)] + [(1, t, 1) for t in range(NT)]
          + [(2, t, 0) for t in range(NT)])
CELLS = {(0, 0): [(0, 0), (1, 4)], (0, 1): [(0, 2)],
         (1, 1): [(1, 0), (2, 4), (3, 2)],
         (2, 0): [(2, 0), (3, 4)]}


def make_steps():
    steps = []
    piece = {key: n for n, key in enumerate(PIECES)}

    def products(ph, t):
        out = []
        for h in ((0, 1) if ph == 0 else (2 - ph,)):
            out += [("product", piece[ph, t, h], c) for c in range(len(CELLS[ph, h]))]
        return out

    def with_gram(parts, pair, rounds):
        out = []
        for n, part in enumerate(parts):
            out.append(part)
            if n < len(rounds):
                out.append(("gram", pair, rounds[n]))
        return out

    steps += [("transpose", 0, 0), ("transpose", 0, 1)]
    for t in range(ZT - 2):
        steps += products(0, t) + [("transpose", 0, t + 2)]
    steps += with_gram(products(0, ZT - 2) + products(0, ZT - 1), 0, range(6))
    steps += [("gram", 0, 6), ("gram", 0, 7), ("bounce", 0), ("transpose", 1, 0)]
    steps += [("inner", 0, m) for m in range(IT)]
    for m in range(IT):
        steps += products(0, ZT + m) + [("transpose", 1, 1 + m)]
    for t in range(9):
        steps += products(1, t) + [("transpose", 1, t + 4)]
    steps += with_gram([s for t in (9, 10, 11) for s in products(1, t)], 1, range(ROUNDS))
    steps += [("bounce", 1)] + products(1, 12) + [("inner", 1, m) for m in range(IT)]
    for m in range(IT):
        steps += products(1, ZT + m)
    for t in range(NT):
        steps += products(2, t)
    return steps


STEPS = make_steps()
SPLITS = [(s[1], s[2] + (ZT if s[0] == "inner" else 0)) for s in STEPS if s[0] in ("transpose", "inner")]
PRODUCTS = [s[1:] for s in STEPS if s[0] == "product"]
LAST_CELL = {n: len(CELLS[ph, h]) for n, (ph, t, h) in enumerate(PIECES)}


def split_count(pair, t):
    return SPLITS.index((pair, t)) + 1


def transposed_count(pair, t):
    return [s for s in STEPS if s[0] == "transpose"].index(("transpose", pair, t)) + 1


def products_through(n, cell=None):
    return PRODUCTS.index((n, LAST_CELL[n] - 1 if cell is None else cell)) + 1


def aux_before(step):
    uses = {0: [("dense",)], 1: []}
    for s in STEPS:
        if s == step:
            break
        if s[0] == "transpose":
            uses[s[2] % 2].append(s)
        if s[0] == "gram":
            uses[0].append(s)
            uses[1].append(s)
    return uses


def build(nc, x_dense, x_sparse, emb, w1, b1, w2, b2, w_rows, out, gram_dram):
    with ExitStack() as ctx:
        def sb(name, shape, dt):
            return ctx.enter_context(nc.sbuf_tensor(name, shape, dt))

        def sem(name):
            return ctx.enter_context(nc.semaphore(name))

        x_idx = sb("x_idx", [P, BT, FIELDS], I32)
        field_base = sb("field_base", [P, BT, FIELDS], I32)
        wrap = sb("wrap", [P, BT, FIELDS], F32)
        wrapped = sb("wrapped", [P, BT, FIELDS], F32)
        clamped = sb("clamped", [P, BT, FIELDS], F32)
        row_idx = sb("row_idx", [P, BT, FIELDS], U32)
        w_row_idx = sb("w_row_idx", [P, IT], U32)
        dense = sb("dense", [P, BT, DENSE + 1], F32)
        ones = sb("ones", [P, P], F32)
        ident = sb("ident", [P, P], F32)
        E = sb("E", [P, ZT, 2, 2, K], F32)
        ET = sb("ET", [P, GROUPS, 4, 32], F32)
        G = sb("G", [P, FIELDS, P], F32)
        x_in = sb("x_in", [P, 2, IT, 2 * P], F32)
        x_hi = sb("x_hi", [P, NT, BATCH], F32R)
        x_lo = sb("x_lo", [P, NT, BATCH], F32R)
        w_raw = sb("w_raw", [P, RAW, HW], F32)
        w_in = sb("w_in", [P, IT, HID], F32)
        w_hi = sb("w_hi", [P, HL, HW], F32R)
        w_lo = sb("w_lo", [P, HL, HW], F32R)
        w2_all = sb("w2_all", [P, HID], F32)
        b2_all = sb("b2_all", [P, 1], F32)
        parts = sb("parts", [P, BT, 4], F32)
        logit = sb("logit", [P, BT], F32)
        result = sb("result", [P, BT], F32)
        bank = [ctx.enter_context(nc.psum_tensor(f"bank{n}", [P, 512], F32)) for n in range(8)]

        idx_landed = sem("idx_landed")
        base_ready = sem("base_ready")
        idx_step = sem("idx_step")
        idx_ready = sem("idx_ready")
        small_landed = sem("small_landed")
        bias_landed = sem("bias_landed")
        consts_landed = sem("consts_landed")
        dense_landed = sem("dense_landed")
        ones_ready = sem("ones_ready")
        ident_ready = sem("ident_ready")
        et_pad_ready = sem("et_pad_ready")
        x_in_zero = sem("x_in_zero")
        w_in_zero = sem("w_in_zero")
        dense_ones = sem("dense_ones")
        w_in_landed = sem("w_in_landed")
        e_landed = [sem(f"e_landed{t}") for t in range(ZT)]
        w_landed = [sem(f"w_landed{n}") for n in range(RAW)]
        dense_transposed = sem("dense_transposed")
        dense_copied = sem("dense_copied")
        e_transposed = sem("e_transposed")
        et0_ready = sem("et0_ready")
        et1_ready = sem("et1_ready")
        x_hi_ready = sem("x_hi_ready")
        x_split = sem("x_split")
        w_hi_ready = sem("w_hi_ready")
        w_split = sem("w_split")
        products_done = sem("products_done")
        drained = sem("drained")
        gram_done = sem("gram_done")
        g0_copied = sem("g0_copied")
        g1_copied = sem("g1_copied")
        g_stored = sem("g_stored")
        x_in_landed = sem("x_in_landed")
        logit_ready = sem("logit_ready")
        result_ready = sem("result_ready")
        out_stored = sem("out_stored")

        emb_rows = emb.rearrange("f v k -> (f v) k")
        gram_store = [gram_dram[pair].rearrange("(i j) b -> i j b", i=FIELDS) for pair in range(2)]
        z_rows = w1[DENSE:DENSE + FIELDS * K, :].rearrange("(t p) n -> t p n", p=P)
        ring = {}
        for n, (ph, t, h) in enumerate(PIECES):
            if t < ZT:
                ring[n] = len(ring)

        def w_source(n):
            ph, t, h = PIECES[n]
            if t < ZT:
                return w_raw[0:P, ring[n] % RAW, 0:HALF_W[h]]
            return w_in[0:KROWS[t], t - ZT, HALF_AT[h]:HALF_AT[h] + HALF_W[h]]

        def w_parts(n):
            ph, t, h = PIECES[n]
            return (w_hi[0:KROWS[t], n % HL, 0:HALF_W[h]], w_lo[0:KROWS[t], n % HL, 0:HALF_W[h]])

        def x_parts(pair, t):
            b = slice(2 * pair * P, (2 * pair + 2) * P)
            return x_hi[0:KROWS[t], t, b], x_lo[0:KROWS[t], t, b]

        def wait_w(eng, n):
            if PIECES[n][1] < ZT:
                eng.wait_ge(w_landed[ring[n] % RAW], 16 * (ring[n] // RAW + 1))
            else:
                eng.wait_ge(w_in_landed, 16 * IT)
                eng.wait_ge(bias_landed, 32)

        def et_view(src, r, f):
            return src[64 * f:64 * f + 64, r * P:(r + 1) * P].rearrange("k (s g) -> k s g", s=4)

        def et_place(r, t, f):
            return ET[64 * r:64 * r + 64, :, :, 2 * t + f].rearrange("k g s -> k s g")

        def gram_view(src, s):
            v = src[32 * s:32 * s + FIELDS, 0:PER_BANK * 4 * FIELDS]
            return v.rearrange("i (g s j) -> i g s j", g=PER_BANK, s=4)[:, :, s, :]

        def gram_place(r, s, rnd):
            v = G[32 * r:32 * r + FIELDS, :, 32 * s + PER_BANK * rnd:32 * s + PER_BANK * (rnd + 1)]
            return v.rearrange("i j g -> i g j")

        first_use = {}
        last_use = {}
        for k, (n, c) in enumerate(PRODUCTS):
            ph, t, h = PIECES[n]
            bt, b0 = CELLS[ph, h][c]
            if t == 0:
                first_use[k] = (ph, b0)
            if t == NT - 1:
                last_use[k] = (ph, b0)
        drain_order = [last_use[k] for k in sorted(last_use)]

        block = ctx.enter_context(nc.Block())

        @block.sync
        def _(sp):
            sp.dma_start(x_idx[:], x_sparse.rearrange("(p t) f -> p t f", t=BT)).then_inc(idx_landed, 16)

            def load(n):
                if n not in ring:
                    return
                ph, t, h = PIECES[n]
                if ring[n] >= RAW:
                    before = next(m for m in ring if ring[m] == ring[n] - RAW)
                    sp.wait_ge(w_split, before + 1)
                sp.dma_start(w_source(n), z_rows[t, :, HALF_AT[h]:HALF_AT[h] + HALF_W[h]])\
                  .then_inc(w_landed[ring[n] % RAW], 16)

            for n in range(FETCH):
                load(n)
                if n == 1:
                    sp.wait_ge(w_in_zero, 1)
                    last = NT - 1 - ZT
                    sp.dma_start(w_in[DENSE_AT:DENSE_AT + DENSE, last, :], w1[0:DENSE, :])\
                      .then_inc(bias_landed, 16)
                    sp.dma_start(w_in[DENSE_AT + DENSE:DENSE_AT + DENSE + 1, last, :],
                                 b1.rearrange("(a n) -> a n", a=1)).then_inc(bias_landed, 16)
            for step in STEPS:
                if step[0] == "product" and step[2] == 0 and step[1] + FETCH < len(PIECES):
                    load(step[1] + FETCH)
                if step[0] == "bounce":
                    pair = step[1]
                    sp.wait_ge(g0_copied, ROUNDS * (pair + 1))
                    sp.wait_ge(g1_copied, ROUNDS * (pair + 1))
                    for r in range(2):
                        sp.dma_start(gram_store[pair][:, :, r * P:(r + 1) * P], G[32 * r:32 * r + FIELDS])\
                          .then_inc(g_stored, 16)
                    sp.wait_ge(g_stored, 32 * (pair + 1))
                    sp.wait_ge(x_in_zero, 1)
                    a0 = 0
                    for m in range(IT):
                        n = BLOCK_A[m]
                        lo = (FIELDS + 1) * a0 + 1
                        rows = gram_dram[pair, lo:lo + n * (FIELDS + 1), :] if m < IT - 1 else None
                        if rows is None:
                            lead = gram_dram[pair, lo - 1:lo - 1 + n * (FIELDS + 1), :]
                            src = lead.rearrange("(a d) b -> a d b", a=n)[:, 1:1 + HALF, :]
                        else:
                            src = rows.rearrange("(a d) b -> a d b", a=n)[:, 0:HALF, :]
                        sp.dma_start(x_in[0:INNER[m], pair, m, :], src).then_inc(x_in_landed, 16)
                        a0 += n
            sp.wait_ge(result_ready, 1)
            sp.dma_start(out.rearrange("(p t) o -> p (t o)", t=BT), result[:]).then_inc(out_stored, 16)
            sp.wait_ge(out_stored, 16)

        @block.gpsimd
        def _(pool):
            nc.gpsimd.iota(field_base[:], [[0, BT], [VOCAB, FIELDS]], base=0, channel_multiplier=0)\
              .then_inc(base_ready, 1)
            nc.gpsimd.memset(ones[:], 1.0).then_inc(ones_ready, 1)
            pool.wait_ge(ones_ready, 1)
            nc.gpsimd.affine_select(out=ident[:], in_=ones[:], compare_op=ALU.is_equal, fill=0.0, base=0,
                                    pattern=[[-1, P]], channel_multiplier=1).then_inc(ident_ready, 1)
            pool.wait_ge(idx_ready, 1)
            for pair in range(2):
                for t in range(ZT):
                    if pair == 1:
                        pool.wait_ge(e_transposed, transposed_count(0, t))
                    for r in range(2):
                        for f in range(2):
                            at = row_idx[:, 2 * pair + r, 2 * t + f:2 * t + f + 1]
                            nc.gpsimd.indirect_dma_start(
                                out=E[:, t, r, f, :], out_offset=None, in_=emb_rows,
                                in_offset=bass.IndirectOffsetOnAxis(ap=at, axis=0)).then_inc(e_landed[t], 16)
                    if pair == 0 and t == ZT // 2:
                        pool.wait_ge(small_landed, 16)
                        pool.wait_ge(w_in_zero, 1)
                        for m in range(IT):
                            nc.gpsimd.indirect_dma_start(
                                out=w_in[0:INNER[m], m, :], out_offset=None, in_=w1,
                                in_offset=bass.IndirectOffsetOnAxis(ap=w_row_idx[0:INNER[m], m:m + 1], axis=0))\
                              .then_inc(w_in_landed, 16)

        @block.scalar
        def _(act):
            act.dma_start(dense[:, :, 0:DENSE], x_dense.rearrange("(p t) d -> p t d", t=BT),
                          ).then_inc(dense_landed, 16)
            act.dma_start(w_row_idx[:], w_rows).then_inc(small_landed, 16)
            act.dma_start(w2_all[:], w2.rearrange("n o -> (o n)").partition_broadcast(P)).then_inc(consts_landed, 16)
            act.dma_start(b2_all[:], b2.partition_broadcast(P)).then_inc(consts_landed, 16)

            def split_w(n):
                wait_w(act, n)
                if n >= HL:
                    act.wait_ge(products_done, products_through(n - HL))
                nc.scalar.copy(w_parts(n)[0], w_source(n)).then_inc(w_hi_ready, 1)

            for n in range(LEAD):
                split_w(n)
            act.wait_ge(dense_transposed, 1)
            act.wait_ge(x_in_zero, 1)
            nc.scalar.copy(x_in[DENSE_AT:DENSE_AT + DENSE + 1, :, IT - 1, :],
                           bank[AUX][0:DENSE + 1, :].rearrange("p (a b) -> p a b", a=2)).then_inc(dense_copied, 1)
            nx = ntr = ngr = 0
            for step in STEPS:
                if step[0] == "product" and step[2] == 0 and step[1] + LEAD < len(PIECES):
                    split_w(step[1] + LEAD)
                if step[0] == "transpose":
                    pair, t = step[1:]
                    src = bank[AUX + t % 2]
                    ntr += 1
                    act.wait_ge(e_transposed, ntr)
                    if pair == 1 and t == 0:
                        act.wait_ge(gram_done, ROUNDS)
                    for f in range(2):
                        nc.scalar.copy(et_place(0, t, f), et_view(src, 0, f)).then_inc(et0_ready, 1)
                    nc.scalar.copy(x_parts(pair, t)[0], src[:, 0:2 * P]).then_inc(x_hi_ready, 1)
                if step[0] == "gram":
                    ngr += 1
                    act.wait_ge(gram_done, ngr)
                    if step[2] == 0 and step[1] == 1:
                        act.wait_ge(g_stored, 32)
                    for s in range(4):
                        last = nc.scalar.copy(gram_place(0, s, step[2]), gram_view(bank[AUX], s))
                    last.then_inc(g0_copied, 1)
                if step[0] == "inner":
                    pair, m = step[1:]
                    act.wait_ge(x_in_landed, 16 * IT * (pair + 1))
                    if m == IT - 1:
                        act.wait_ge(dense_copied, 1)
                    nc.scalar.copy(x_parts(pair, ZT + m)[0], x_in[0:KROWS[ZT + m], pair, m, :])\
                      .then_inc(x_hi_ready, 1)
            act.wait_ge(logit_ready, 1)
            act.wait_ge(consts_landed, 32)
            nc.scalar.activation(result[:], logit[:], ACT.Sigmoid, bias=b2_all[:, 0:1]).then_inc(result_ready, 1)

        @block.vector
        def _(dve):
            nc.vector.memset(x_in[64:P, :, IT - 1, :], 0.0).then_inc(x_in_zero, 1)
            nc.vector.memset(w_in[64:P, IT - 1, :], 0.0).then_inc(w_in_zero, 1)
            nc.vector.memset(ET[:, :, :, FIELDS:32], 0.0).then_inc(et_pad_ready, 1)
            nc.vector.memset(dense[:, :, DENSE:DENSE + 1], 1.0).then_inc(dense_ones, 1)
            dve.wait_ge(idx_landed, 16)
            nc.vector.tensor_scalar(wrap[:], x_idx[:], 0.0, float(VOCAB), ALU.is_lt, ALU.mult).then_inc(idx_step, 1)
            dve.wait_ge(idx_step, 1)
            nc.vector.tensor_tensor(wrapped[:], x_idx[:], wrap[:], ALU.add).then_inc(idx_step, 1)
            dve.wait_ge(idx_step, 2)
            nc.vector.tensor_scalar(clamped[:], wrapped[:], 0.0, float(VOCAB - 1), ALU.max, ALU.min)\
              .then_inc(idx_step, 1)
            dve.wait_ge(idx_step, 3)
            dve.wait_ge(base_ready, 1)
            nc.vector.tensor_tensor(row_idx[:], clamped[:], field_base[:], ALU.add).then_inc(idx_ready, 1)

            def split_w(n):
                dve.wait_ge(w_hi_ready, n + 1)
                hi, lo = w_parts(n)
                nc.vector.tensor_tensor(lo, w_source(n), hi.bitcast(F32), ALU.subtract).then_inc(w_split, 1)

            def drain(k):
                n, c = PRODUCTS[k]
                ph, t, h = PIECES[n]
                bt, b0 = CELLS[ph, h][c]
                dve.wait_ge(products_done, k + 1)
                for q, (at, width) in enumerate(CHUNKS[h]):
                    nc.vector.scalar_tensor_tensor(
                        out=bank[b0 + q][:, 0:width], in0=bank[b0 + q][:, 0:width], scalar=0.0,
                        in1=w2_all[:, at:at + width], op0=ALU.max, op1=ALU.mult,
                        accum_out=parts[:, bt, 2 * h + q:2 * h + q + 1]).then_inc(drained, 1)

            for n in range(LEAD):
                split_w(n)
            nx = ngr = k = 0
            for step in STEPS:
                if step[0] == "product":
                    if step[2] == 0 and step[1] + LEAD < len(PIECES):
                        split_w(step[1] + LEAD)
                    if k in last_use:
                        if k == min(last_use):
                            dve.wait_ge(consts_landed, 32)
                        drain(k)
                    k += 1
                if step[0] == "transpose":
                    pair, t = step[1:]
                    nx += 1
                    dve.wait_ge(x_hi_ready, nx)
                    hi, lo = x_parts(pair, t)
                    nc.vector.tensor_tensor(lo, bank[AUX + t % 2][:, 0:2 * P], hi.bitcast(F32), ALU.subtract)\
                      .then_inc(x_split, 1)
                    if pair == 1 and t == 0:
                        dve.wait_ge(gram_done, ROUNDS)
                    for f in range(2):
                        nc.vector.tensor_copy(et_place(1, t, f), et_view(bank[AUX + t % 2], 1, f))\
                          .then_inc(et1_ready, 1)
                if step[0] == "gram":
                    ngr += 1
                    dve.wait_ge(gram_done, ngr)
                    if step[2] == 0 and step[1] == 1:
                        dve.wait_ge(g_stored, 32)
                    for s in range(4):
                        last = nc.vector.tensor_copy(gram_place(1, s, step[2]), gram_view(bank[AUX + 1], s))
                    last.then_inc(g1_copied, 1)
                if step[0] == "inner":
                    pair, m = step[1:]
                    nx += 1
                    dve.wait_ge(x_hi_ready, nx)
                    hi, lo = x_parts(pair, ZT + m)
                    nc.vector.tensor_tensor(lo, x_in[0:KROWS[ZT + m], pair, m, :], hi.bitcast(F32), ALU.subtract)\
                      .then_inc(x_split, 1)
            dve.wait_ge(drained, 2 * len(drain_order))
            nc.vector.tensor_reduce(logit[:], parts[:], AX.X, ALU.add).then_inc(logit_ready, 1)

        @block.tensor
        def _(pe):
            pe.wait_ge(ident_ready, 1)
            pe.wait_ge(dense_landed, 16)
            pe.wait_ge(dense_ones, 1)
            for bt in range(BT):
                last = nc.tensor.transpose(bank[AUX][0:DENSE + 1, bt * P:(bt + 1) * P], dense[:, bt, :], ident[:])
            last.then_inc(dense_transposed, 1)
            seen = [0] * ZT

            def wait_aux(step, b):
                before = aux_before(step)[b]
                if not before:
                    return
                s = before[-1]
                if s[0] == "dense":
                    pe.wait_ge(dense_copied, 1)
                elif s[0] == "transpose":
                    pe.wait_ge(et1_ready, 2 * transposed_count(s[1], s[2]))
                else:
                    pe.wait_ge((g0_copied, g1_copied)[b], ROUNDS * s[1] + s[2] + 1)

            k = 0
            for step in STEPS:
                if step[0] == "transpose":
                    pair, t = step[1:]
                    pe.wait_ge(e_landed[t], 64 * (pair + 1))
                    wait_aux(step, t % 2)
                    dst = bank[AUX + t % 2]
                    for r in range(2):
                        last = nc.tensor.transpose(dst[:, r * P:(r + 1) * P],
                                                   E[:, t, r, :, :].rearrange("p f k -> p (f k)"), ident[:])
                    last.then_inc(e_transposed, 1)
                if step[0] == "gram":
                    pair, rnd = step[1:]
                    wait_aux(step, 0)
                    wait_aux(step, 1)
                    if rnd == 0:
                        pe.wait_ge(et0_ready, FIELDS * (pair + 1))
                        pe.wait_ge(et1_ready, FIELDS * (pair + 1))
                        if pair == 0:
                            pe.wait_ge(et_pad_ready, 1)
                    for q in range(PER_BANK):
                        for r in range(2):
                            e = ET[64 * r:64 * r + 64, PER_BANK * rnd + q]
                            last = nc.tensor.matmul(
                                bank[AUX + r][:, q * 4 * FIELDS:(q + 1) * 4 * FIELDS],
                                e.rearrange("k s f -> k (s f)"), e[:, :, 0:FIELDS], start=True, stop=True)
                    last.then_inc(gram_done, 1)
                if step[0] == "product":
                    n, c = step[1:]
                    ph, t, h = PIECES[n]
                    bt, b0 = CELLS[ph, h][c]
                    if c == 0:
                        pe.wait_ge(w_split, n + 1)
                    pe.wait_ge(x_split, split_count(bt // 2, t))
                    if t == 0 and ph > 0:
                        pe.wait_ge(drained, 2 * (drain_order.index((ph - 1, b0)) + 1))
                    hi, lo = w_parts(n)
                    xh = x_hi[0:KROWS[t], t, bt * P:(bt + 1) * P]
                    xl = x_lo[0:KROWS[t], t, bt * P:(bt + 1) * P]
                    for m, (x, w) in enumerate(((xh, hi), (xh, lo), (xl, hi))):
                        for q, (at, width) in enumerate(CHUNKS[h]):
                            cols = slice(at - HALF_AT[h], at - HALF_AT[h] + width)
                            last = nc.tensor.matmul(bank[b0 + q][:, 0:width], x, w[:, cols],
                                                    start=(t == 0 and m == 0), stop=(t == NT - 1 and m == 2))
                    last.then_inc(products_done, 1)
                    k += 1


def kernel(r_x_dense, r_x_sparse, L0_rec_emb_tables, L0_rec_w1, L0_rec_b1, L0_rec_w2, L0_rec_b2):
    import numpy as np
    import concourse.bacc as bacc
    from concourse.bass_utils import run_bass_kernel_spmd

    triu = {}
    for i in range(FIELDS):
        for j in range(i + 1, FIELDS):
            triu[i, j] = DENSE + FIELDS * K + len(triu)
    w_rows = np.zeros((P, IT), np.uint32)
    a0 = 0
    for m, n in enumerate(BLOCK_A):
        for a in range(n):
            for d in range(HALF):
                i, j = divmod((FIELDS + 1) * (a0 + a) + d + 1, FIELDS)
                w_rows[a * HALF + d, m] = triu[min(i, j), max(i, j)]
        a0 += n

    arrays = {
        "x_dense": np.ascontiguousarray(r_x_dense), "x_sparse": np.ascontiguousarray(r_x_sparse),
        "emb": np.ascontiguousarray(L0_rec_emb_tables), "w1": np.ascontiguousarray(L0_rec_w1),
        "b1": np.ascontiguousarray(L0_rec_b1), "w2": np.ascontiguousarray(L0_rec_w2),
        "b2": np.ascontiguousarray(L0_rec_b2), "w_rows": w_rows,
    }
    nc = bacc.Bacc("TRN2", target_bir_lowering=False, num_devices=1)
    args = [nc.dram_tensor(name, a.shape, mybir.dt.from_np(a.dtype), kind="ExternalInput").ap()
            for name, a in arrays.items()]
    out = nc.dram_tensor("out", (BATCH, 1), F32, kind="ExternalOutput").ap()
    gram_dram = nc.dram_tensor("gram_dram", (2, ROWS_G, 2 * P), F32, kind="Internal").ap()
    build(nc, *args, out, gram_dram)
    return run_bass_kernel_spmd(nc, [arrays], core_ids=[0]).results[0]["out"]
```

```python
from contextlib import ExitStack

import concourse.bass as bass
from concourse import mybir

ALU = mybir.AluOpType
ACT = mybir.ActivationFunctionType
AX = mybir.AxisListType
F32 = mybir.dt.float32
F32R = mybir.dt.float32r
I32 = mybir.dt.int32
U32 = mybir.dt.uint32

P = 128
BATCH, DENSE, FIELDS, VOCAB, K = 512, 13, 26, 6250, 64
PAIRS = FIELDS * (FIELDS - 1) // 2
HID = DENSE + FIELDS * K + PAIRS
BT = BATCH // P

ZT = FIELDS // 2
ROWS_G = FIELDS * FIELDS
HALF = FIELDS // 2
BLOCK_A = [9, 9, 7]
INNER = [n * HALF for n in BLOCK_A]
IT = len(BLOCK_A)
NT = ZT + IT
INNER_AT = [0, 0, DENSE]
ONES_AT = DENSE + INNER[-1]
KROWS = [P] * ZT + INNER[:-1] + [ONES_AT + 1]

CHUNKS = [[(0, 502), (502, 500)], [(1002, 500), (1502, 500)]]
HALF_AT = [0, 1002]
HALF_W = [1002, 1000]
HW = max(HALF_W)

RAW = 5
HL = 5
GROUPS = P // 4
PER_BANK = 4
ROUNDS = GROUPS // PER_BANK
AUX = 6
LEAD = 3
WARM = 20
PACED = 8
FETCH = 14

PIECES = ([(0, t, h) for t in range(ZT) for h in (0, 1)]
          + [(0, t, h) for h in (1, 0) for t in range(ZT, NT)]
          + [(1, t, 1) for t in range(NT)] + [(2, t, 0) for t in range(NT)])
PIECE = {key: n for n, key in enumerate(PIECES)}
CELLS = {(0, 0): {0: 0, 1: 4}, (0, 1): {0: 2},
         (1, 1): {1: 0, 2: 2, 3: 4},
         (2, 0): {2: 0, 3: 2}}
RINGED = [n for n, (ph, t, h) in enumerate(PIECES) if t < ZT]


def products(ph, t):
    return [("product", PIECE[ph, t, h], bt) for h in ((0, 1) if ph == 0 else (2 - ph,)) for bt in CELLS[ph, h]]


def inner_products(ph, h, bt):
    return [("product", PIECE[ph, t, h], bt) for t in range(ZT, NT)]


def mixed(a, b):
    out = []
    for n in range(max(len(a), len(b))):
        out += a[n:n + 1] + b[n:n + 1]
    return out


def make_steps():
    def gram(bt):
        return [("gram", bt, rnd) for rnd in range(ROUNDS)]

    todo = [("transpose", 0, 0)]
    for t in range(ZT - 1):
        p = products(0, t)
        todo += p[:1] + [("transpose", 0, t + 1)] + p[1:]
    p = [todo.pop()] + products(0, ZT - 1)
    g = gram(0) + [("bounce", 0)] + gram(1) + [("bounce", 1)]
    todo += [("constants",)] + g[:3] + p[:1] + g[3:6] + p[1:2] + g[6:10] + p[2:3] + g[10:14] + p[3:4] + g[14:15] + [("inner", 0)] + g[15:]
    todo += inner_products(0, 1, 0)
    todo += mixed(inner_products(0, 0, 0), [("transpose", 1, 0), ("inner", 1)])
    todo += mixed(inner_products(0, 0, 1), [("transpose", 1, t) for t in (1, 2, 3)])
    for t in range(ZT - 4):
        p = products(1, t)
        todo += p[:-1] + [("transpose", 1, t + 4)] + p[-1:]
    p = [s for t in range(ZT - 4, ZT) for s in products(1, t)]
    for bt in (2, 3):
        g = gram(bt)
        for n in range(0, ROUNDS, 2):
            todo += [p.pop(0)] + g[n:n + 2]
        todo += [("bounce", bt)]
    todo += p[:4] + [("inner", 2)] + p[4:]
    todo += inner_products(1, 1, 1) + inner_products(1, 1, 2)[:1] + [("inner", 3)]
    todo += inner_products(1, 1, 2)[1:] + inner_products(1, 1, 3)
    todo += [s for t in range(NT) for s in products(2, t)]

    steps, begun, split, loaded = [], 1 - LEAD, 0, 0
    left = [len(CELLS[ph, h]) for ph, t, h in PIECES]
    done = []
    for step in todo:
        if step[0] == "product":
            begun = max(begun, step[1])
        while True:
            if (split < min(begun + LEAD, len(PIECES) - 1) + 1 and (split < HL or left[split - HL] == 0)
                    and SPLIT_AFTER.get(split, step) in done + [step]
                    and (split not in RINGED or RINGED.index(split) < loaded)):
                steps.append(("split", split))
                split += 1
            elif (loaded < len(RINGED) and RINGED[loaded] <= begun + FETCH
                  and (loaded < RAW or RINGED[loaded - RAW] < split)):
                steps.append(("load", loaded))
                loaded += 1
            else:
                break
        steps.append(step)
        if step[0] == "product":
            left[step[1]] -= 1
        done.append(step)
    return steps


SPLIT_AFTER = {PIECE[0, ZT, 1]: ("gram", 1, 0), PIECE[0, ZT + 1, 1]: ("gram", 1, 4), PIECE[0, ZT + 2, 1]: ("bounce", 1)}
STEPS = make_steps()
PRODUCTS = [s[1:] for s in STEPS if s[0] == "product"]
TRANSPOSES = [s[1:] for s in STEPS if s[0] == "transpose"]
SPLITS = [s for s in STEPS if s[0] in ("transpose", "inner")]
GRAMS = [s[1:] for s in STEPS if s[0] == "gram"]
AUX_USES = [[s for s in STEPS if s[0] in ("transpose", "gram") and s[2] % 2 == b] for b in range(2)]
COMPLETE = {}
for _k, (_n, _bt) in enumerate(PRODUCTS):
    if PIECES[_n][1] == NT - 1:
        COMPLETE[_k] = (PIECES[_n][0], CELLS[PIECES[_n][0], PIECES[_n][2]][_bt])
DRAINS = list(COMPLETE.values())


def split_count(bt, t):
    return SPLITS.index(("transpose", bt // 2, t) if t < ZT else ("inner", bt)) + 1


def transposed_count(pair, t):
    return TRANSPOSES.index((pair, t)) + 1


def gram_count(bt, rnd):
    return GRAMS.index((bt, rnd)) + 1


def products_through(n):
    return max(k for k, p in enumerate(PRODUCTS) if p[0] == n) + 1


def build(nc, x_dense, x_sparse, emb, w1, b1, w2, b2, w_rows, out, gram_dram):
    with ExitStack() as ctx:
        def sb(name, shape, dt):
            return ctx.enter_context(nc.sbuf_tensor(name, shape, dt))

        def sem(name):
            return ctx.enter_context(nc.semaphore(name))

        x_idx = sb("x_idx", [P, BT, FIELDS], I32)
        field_base = sb("field_base", [P, BT, FIELDS], I32)
        wrap = sb("wrap", [P, BT, FIELDS], F32)
        wrapped = sb("wrapped", [P, BT, FIELDS], F32)
        row_idx = sb("row_idx", [P, BT, FIELDS], U32)
        w_row_idx = sb("w_row_idx", [P, IT], U32)
        dense = sb("dense", [P, BT, DENSE], F32)
        ones = sb("ones", [P, P], F32)
        ident = sb("ident", [P, P], F32)
        E = sb("E", [P, ZT, 2, 2, K], F32)
        ET = sb("ET", [P, GROUPS, 4, 32], F32)
        G = sb("G", [P, FIELDS, P], F32)
        x_in = sb("x_in", [P, BT, IT, P], F32)
        x_hi = sb("x_hi", [P, NT, BATCH], F32R)
        x_lo = sb("x_lo", [P, NT, BATCH], F32R)
        w_raw = sb("w_raw", [P, RAW, HW], F32)
        w_in = sb("w_in", [P, IT, HID], F32)
        w_hi = sb("w_hi", [P, HL, HW], F32R)
        w_lo = sb("w_lo", [P, HL, HW], F32R)
        w2_all = sb("w2_all", [P, HID], F32)
        b2_all = sb("b2_all", [P, 1], F32)
        parts = sb("parts", [P, BT, 4], F32)
        logit = sb("logit", [P, BT], F32)
        result = sb("result", [P, BT], F32)
        bank = [ctx.enter_context(nc.psum_tensor(f"bank{n}", [P, 512], F32)) for n in range(8)]

        idx_landed = sem("idx_landed")
        base_ready = sem("base_ready")
        idx_step = sem("idx_step")
        idx_ready = sem("idx_ready")
        w_row_idx_landed = sem("w_row_idx_landed")
        bias_landed = sem("bias_landed")
        consts_landed = sem("consts_landed")
        dense_landed = sem("dense_landed")
        ones_ready = sem("ones_ready")
        ident_ready = sem("ident_ready")
        et_pad_ready = sem("et_pad_ready")
        ones_row_ready = sem("ones_row_ready")
        w_in_landed = sem("w_in_landed")
        e_landed = [[sem(f"e_landed{t}_{r}") for r in range(2)] for t in range(ZT)]
        w_landed = [sem(f"w_landed{n}") for n in range(RAW)]
        dense_transposed = sem("dense_transposed")
        dense_copied = sem("dense_copied")
        e_transposed = sem("e_transposed")
        et0_ready = sem("et0_ready")
        et1_ready = sem("et1_ready")
        x_hi_ready = sem("x_hi_ready")
        x_split = sem("x_split")
        w_hi_ready = sem("w_hi_ready")
        w_split = sem("w_split")
        products_done = sem("products_done")
        drained = sem("drained")
        gram_done = sem("gram_done")
        g_copied_act = sem("g_copied_act")
        g_copied_dve = sem("g_copied_dve")
        g_stored = sem("g_stored")
        x_in_landed = [sem(f"x_in_landed{bt}") for bt in range(BT)]
        logit_ready = sem("logit_ready")
        result_ready = sem("result_ready")
        out_stored = sem("out_stored")

        emb_rows = emb.rearrange("f v k -> (f v) k")
        z_rows = w1[DENSE:DENSE + FIELDS * K, :].rearrange("(t p) n -> t p n", p=P)

        def w_source(n):
            ph, t, h = PIECES[n]
            if t < ZT:
                return w_raw[0:P, RINGED.index(n) % RAW, 0:HALF_W[h]]
            return w_in[0:KROWS[t], t - ZT, HALF_AT[h]:HALF_AT[h] + HALF_W[h]]

        def w_parts(n):
            ph, t, h = PIECES[n]
            return (w_hi[0:KROWS[t], n % HL, 0:HALF_W[h]], w_lo[0:KROWS[t], n % HL, 0:HALF_W[h]])

        def x_parts(pair, t):
            b = slice(2 * pair * P, (2 * pair + 2) * P)
            return x_hi[:, t, b], x_lo[:, t, b]

        INNER_PARTS = [(KROWS[ZT], slice(0, IT - 1)), (KROWS[NT - 1], slice(IT - 1, IT))]

        def x_inner_parts(bt, rows, tiles):
            b = slice(bt * P, (bt + 1) * P)
            return [x[0:rows, ZT + tiles.start:ZT + tiles.stop, b] for x in (x_hi, x_lo)]

        def et_view(src, r, f):
            return src[64 * f:64 * f + 64, r * P:(r + 1) * P].rearrange("k (s g) -> k s g", s=4)

        def et_place(r, t, f):
            return ET[64 * r:64 * r + 64, :, :, 2 * t + f].rearrange("k g s -> k s g")

        def gram_view(src, s):
            v = src[32 * s:32 * s + FIELDS, 0:PER_BANK * 4 * FIELDS]
            return v.rearrange("i (g s j) -> i g s j", g=PER_BANK, s=4)[:, :, s, :]

        def gram_place(r, s, rnd):
            v = G[32 * r:32 * r + FIELDS, :, 32 * s + PER_BANK * rnd:32 * s + PER_BANK * (rnd + 1)]
            return v.rearrange("i j g -> i g j")

        block = ctx.enter_context(nc.Block())

        @block.sync
        def _(sp):
            sp.dma_start(x_idx[:], x_sparse.rearrange("(p t) f -> p t f", t=BT)).then_inc(idx_landed, 16)
            for step in STEPS:
                if step[0] == "load":
                    m = step[1]
                    ph, t, h = PIECES[RINGED[m]]
                    if 3 <= m < PACED:
                        sp.wait_ge(e_landed[(m - 3) // 2][(m - 3) % 2], 32)
                    if m >= RAW:
                        sp.wait_ge(w_split, RINGED[m - RAW] + 1)
                    sp.dma_start(w_source(RINGED[m]), z_rows[t, :, HALF_AT[h]:HALF_AT[h] + HALF_W[h]])\
                      .then_inc(w_landed[m % RAW], 16)
                    if m == 2 * RAW:
                        sp.dma_start(w_in[ONES_AT:ONES_AT + 1, IT - 1, :], b1.rearrange("(a n) -> a n", a=1))\
                          .then_inc(bias_landed, 16)
                if step[0] == "constants":
                    sp.dma_start(w2_all[:], w2.rearrange("n o -> (o n)").partition_broadcast(P))\
                      .then_inc(consts_landed, 16)
                    sp.dma_start(b2_all[:], b2.partition_broadcast(P)).then_inc(consts_landed, 16)
                if step[0] == "bounce":
                    bt = step[1]
                    r = bt % 2
                    sp.wait_ge(g_copied_act, gram_count(bt, ROUNDS - 1))
                    sp.wait_ge(g_copied_dve, gram_count(bt, ROUNDS - 1))
                    sp.dma_start(gram_dram[bt].rearrange("(i j) b -> i j b", i=FIELDS), G[32 * r:32 * r + FIELDS])\
                      .then_inc(g_stored, 16)
                    sp.wait_ge(g_stored, 16 * (bt + 1))
                    if bt == 0:
                        sp.wait_ge(ones_row_ready, 1)
                    a0 = 0
                    for m, n in enumerate(BLOCK_A):
                        flat = gram_dram[bt, (FIELDS + 1) * a0:(FIELDS + 1) * (a0 + n), :]
                        sp.dma_start(x_in[INNER_AT[m]:INNER_AT[m] + INNER[m], bt, m, :],
                                     flat.rearrange("(a d) b -> a d b", a=n)[:, 1:1 + HALF, :])\
                          .then_inc(x_in_landed[bt], 16)
                        a0 += n
            sp.wait_ge(result_ready, 1)
            sp.dma_start(out.rearrange("(p t) o -> p (t o)", t=BT), result[:]).then_inc(out_stored, 16)
            sp.wait_ge(out_stored, 16)

        @block.gpsimd
        def _(pool):
            nc.gpsimd.iota(field_base[:], [[0, BT], [VOCAB, FIELDS]], base=0, channel_multiplier=0)\
              .then_inc(base_ready, 1)
            nc.gpsimd.memset(ones[:], 1.0).then_inc(ones_ready, 1)
            nc.gpsimd.memset(ET[:, :, :, FIELDS:32], 0.0).then_inc(et_pad_ready, 1)
            pool.wait_ge(ones_ready, 1)
            nc.gpsimd.affine_select(out=ident[:], in_=ones[:], compare_op=ALU.is_equal, fill=0.0, base=0,
                                    pattern=[[-1, P]], channel_multiplier=1).then_inc(ident_ready, 1)
            pool.wait_ge(idx_ready, 1)
            for pair in range(2):
                for t in range(ZT):
                    if pair == 1:
                        pool.wait_ge(e_transposed, transposed_count(0, t))
                    for r in range(2):
                        for f in range(2):
                            at = row_idx[:, 2 * pair + r, 2 * t + f:2 * t + f + 1]
                            nc.gpsimd.indirect_dma_start(
                                out=E[:, t, r, f, :], out_offset=None, in_=emb_rows,
                                in_offset=bass.IndirectOffsetOnAxis(ap=at, axis=0)).then_inc(e_landed[t][r], 16)
                if pair == 0:
                    pool.wait_ge(w_row_idx_landed, 16)
                    for m in range(IT):
                        n = INNER_AT[m] + INNER[m]
                        nc.gpsimd.indirect_dma_start(
                            out=w_in[0:n, m, :], out_offset=None, in_=w1,
                            in_offset=bass.IndirectOffsetOnAxis(ap=w_row_idx[0:n, m:m + 1], axis=0))\
                          .then_inc(w_in_landed, 16)

        @block.scalar
        def _(act):
            act.dma_start(dense[:], x_dense.rearrange("(p t) d -> p t d", t=BT))\
               .then_inc(dense_landed, 16)
            act.dma_start(w_row_idx[:], w_rows).then_inc(w_row_idx_landed, 16)
            act.wait_ge(dense_transposed, 1)
            nc.scalar.copy(x_in[0:DENSE, :, IT - 1, :],
                           bank[AUX][0:DENSE, :].rearrange("p (a b) -> p a b", a=BT)).then_inc(dense_copied, 1)
            for step in STEPS:
                if step[0] == "split":
                    n = step[1]
                    if PIECES[n][1] < ZT:
                        m = RINGED.index(n)
                        act.wait_ge(w_landed[m % RAW], 16 * (m // RAW + 1))
                    else:
                        act.wait_ge(w_in_landed, 16 * IT)
                        act.wait_ge(bias_landed, 16)
                    if n >= HL:
                        act.wait_ge(products_done, products_through(n - HL))
                    nc.scalar.copy(w_parts(n)[0], w_source(n)).then_inc(w_hi_ready, 1)
                if step[0] == "transpose":
                    pair, t = step[1:]
                    src = bank[AUX + t % 2]
                    act.wait_ge(e_transposed, transposed_count(pair, t))
                    nc.scalar.copy(x_parts(pair, t)[0], src[:, 0:2 * P]).then_inc(x_hi_ready, 1)
                    if pair == 1:
                        act.wait_ge(gram_done, gram_count(1, ROUNDS - 1))
                    for r in ((0,), (0, 1))[pair]:
                        for f in range(2):
                            last = nc.scalar.copy(et_place(r, t, f), et_view(src, r, f))
                    last.then_inc(et0_ready, 1)
                if step[0] == "gram":
                    bt, rnd = step[1:]
                    act.wait_ge(gram_done, gram_count(bt, rnd))
                    if bt >= 2:
                        act.wait_ge(g_stored, 16 * (bt - 1))
                    for s in (0, 1):
                        last = nc.scalar.copy(gram_place(bt % 2, s, rnd), gram_view(bank[AUX + rnd % 2], s))
                    last.then_inc(g_copied_act, 1)
                if step[0] == "inner":
                    bt = step[1]
                    act.wait_ge(x_in_landed[bt], 16 * IT)
                    if bt == 0:
                        act.wait_ge(dense_copied, 1)
                        act.wait_ge(ones_row_ready, 1)
                    for rows, tiles in INNER_PARTS:
                        last = nc.scalar.copy(x_inner_parts(bt, rows, tiles)[0], x_in[0:rows, bt, tiles, :])
                    last.then_inc(x_hi_ready, 1)
            act.wait_ge(logit_ready, 1)
            act.wait_ge(consts_landed, 32)
            nc.scalar.activation(result[:], logit[:], ACT.Sigmoid, bias=b2_all[:, 0:1]).then_inc(result_ready, 1)

        @block.vector
        def _(dve):
            dve.wait_ge(idx_landed, 16)
            nc.vector.tensor_scalar(wrap[:], x_idx[:], 0.0, float(VOCAB), ALU.is_lt, ALU.mult).then_inc(idx_step, 1)
            dve.wait_ge(idx_step, 1)
            nc.vector.scalar_tensor_tensor(out=wrapped[:], in0=x_idx[:], scalar=float(VOCAB - 1), in1=wrap[:],
                                           op0=ALU.min, op1=ALU.add).then_inc(idx_step, 1)
            dve.wait_ge(idx_step, 2)
            dve.wait_ge(base_ready, 1)
            nc.vector.scalar_tensor_tensor(out=row_idx[:], in0=wrapped[:], scalar=0.0, in1=field_base[:],
                                           op0=ALU.max, op1=ALU.add).then_inc(idx_ready, 1)
            nc.vector.memset(x_in[96:ONES_AT + 1, :, IT - 1, :], 1.0).then_inc(ones_row_ready, 1)

            for step in STEPS:
                if step[0] == "split":
                    n = step[1]
                    dve.wait_ge(w_hi_ready, n + 1)
                    hi, lo = w_parts(n)
                    nc.vector.tensor_tensor(lo, w_source(n), hi.bitcast(F32), ALU.subtract).then_inc(w_split, 1)
                if step[0] == "transpose":
                    pair, t = step[1:]
                    dve.wait_ge(x_hi_ready, SPLITS.index(step) + 1)
                    dve.wait_ge(et0_ready, transposed_count(pair, t))
                    hi, lo = x_parts(pair, t)
                    nc.vector.tensor_tensor(lo, bank[AUX + t % 2][:, 0:2 * P], hi.bitcast(F32), ALU.subtract)\
                      .then_inc(x_split, 1)
                    if pair == 0:
                        for f in range(2):
                            last = nc.vector.tensor_copy(et_place(1, t, f), et_view(bank[AUX + t % 2], 1, f))
                        last.then_inc(et1_ready, 1)
                if step[0] == "gram":
                    bt, rnd = step[1:]
                    dve.wait_ge(gram_done, gram_count(bt, rnd))
                    if bt >= 2:
                        dve.wait_ge(g_stored, 16 * (bt - 1))
                    for s in (2, 3):
                        last = nc.vector.tensor_copy(gram_place(bt % 2, s, rnd), gram_view(bank[AUX + rnd % 2], s))
                    last.then_inc(g_copied_dve, 1)
                if step[0] == "inner":
                    bt = step[1]
                    dve.wait_ge(x_hi_ready, SPLITS.index(step) + 1)
                    for rows, tiles in INNER_PARTS:
                        hi, lo = x_inner_parts(bt, rows, tiles)
                        last = nc.vector.tensor_tensor(lo, x_in[0:rows, bt, tiles, :], hi.bitcast(F32), ALU.subtract)
                    last.then_inc(x_split, 1)
                if step[0] == "product" and PIECES[step[1]][1] == NT - 1:
                    n, bt = step[1:]
                    ph, t, h = PIECES[n]
                    if (ph, CELLS[ph, h][bt]) == DRAINS[0]:
                        dve.wait_ge(consts_landed, 32)
                    dve.wait_ge(products_done, PRODUCTS.index((n, bt)) + 1)
                    for q, (at, width) in enumerate(CHUNKS[h]):
                        cell = bank[CELLS[ph, h][bt] + q][:, 0:width]
                        nc.vector.scalar_tensor_tensor(
                            out=cell, in0=cell, scalar=0.0, in1=w2_all[:, at:at + width], op0=ALU.max,
                            op1=ALU.mult, accum_out=parts[:, bt, 2 * h + q:2 * h + q + 1]).then_inc(drained, 1)
            dve.wait_ge(drained, 2 * len(DRAINS))
            nc.vector.tensor_reduce(logit[:], parts[:], AX.X, ALU.add).then_inc(logit_ready, 1)

        @block.tensor
        def _(pe):
            pe.wait_ge(ident_ready, 1)
            pe.wait_ge(dense_landed, 16)
            for bt in range(BT):
                last = nc.tensor.transpose(bank[AUX][0:DENSE, bt * P:(bt + 1) * P], dense[:, bt, :], ident[:])
            last.then_inc(dense_transposed, 1)
            for n in range(WARM):
                nc.tensor.matmul(bank[0][:, 0:P], ident[:], ones[:], start=True, stop=True)

            def wait_aux(step):
                uses = AUX_USES[step[2] % 2]
                n = uses.index(step)
                if n == 0:
                    if step[2] % 2 == 0:
                        pe.wait_ge(dense_copied, 1)
                elif uses[n - 1][0] == "transpose":
                    pair, t = uses[n - 1][1:]
                    if pair == 0:
                        pe.wait_ge(et1_ready, transposed_count(pair, t))
                    else:
                        pe.wait_ge(x_split, split_count(2 * pair, t))
                else:
                    pe.wait_ge(g_copied_act, gram_count(*uses[n - 1][1:]))
                    pe.wait_ge(g_copied_dve, gram_count(*uses[n - 1][1:]))

            for step in STEPS:
                if step[0] == "transpose":
                    pair, t = step[1:]
                    wait_aux(step)
                    for r in range(2):
                        pe.wait_ge(e_landed[t][r], 32 * (pair + 1))
                        last = nc.tensor.transpose(bank[AUX + t % 2][:, r * P:(r + 1) * P],
                                                   E[:, t, r, :, :].rearrange("p f k -> p (f k)"), ident[:])
                    last.then_inc(e_transposed, 1)
                if step[0] == "gram":
                    bt, rnd = step[1:]
                    r = bt % 2
                    wait_aux(step)
                    if rnd == 0:
                        if bt == 1:
                            pe.wait_ge(et1_ready, ZT)
                        else:
                            pe.wait_ge(et0_ready, ZT * (bt // 2 + 1))
                        if bt == 0:
                            pe.wait_ge(et_pad_ready, 1)
                    for q in range(PER_BANK):
                        e = ET[64 * r:64 * r + 64, PER_BANK * rnd + q]
                        last = nc.tensor.matmul(
                            bank[AUX + rnd % 2][:, q * 4 * FIELDS:(q + 1) * 4 * FIELDS],
                            e.rearrange("k s f -> k (s f)"), e[:, :, 0:FIELDS], start=True, stop=True)
                    last.then_inc(gram_done, 1)
                if step[0] == "product":
                    n, bt = step[1:]
                    ph, t, h = PIECES[n]
                    b0 = CELLS[ph, h][bt]
                    pe.wait_ge(w_split, n + 1)
                    pe.wait_ge(x_split, split_count(bt, t))
                    if t == 0 and ph > 0:
                        pe.wait_ge(drained, 2 * (DRAINS.index((ph - 1, b0)) + 1))
                    hi, lo = w_parts(n)
                    xh = x_hi[0:KROWS[t], t, bt * P:(bt + 1) * P]
                    xl = x_lo[0:KROWS[t], t, bt * P:(bt + 1) * P]
                    for m, (x, w) in enumerate(((xh, hi), (xh, lo), (xl, hi))):
                        for q, (at, width) in enumerate(CHUNKS[h]):
                            cols = slice(at - HALF_AT[h], at - HALF_AT[h] + width)
                            last = nc.tensor.matmul(bank[b0 + q][:, 0:width], x, w[:, cols],
                                                    start=(t == 0 and m == 0), stop=(t == NT - 1 and m == 2))
                    last.then_inc(products_done, 1)


def kernel(r_x_dense, r_x_sparse, L0_rec_emb_tables, L0_rec_w1, L0_rec_b1, L0_rec_w2, L0_rec_b2):
    import numpy as np
    import concourse.bacc as bacc
    from concourse.bass_utils import run_bass_kernel_spmd

    triu = {}
    for i in range(FIELDS):
        for j in range(i + 1, FIELDS):
            triu[i, j] = DENSE + FIELDS * K + len(triu)
    w_rows = np.zeros((P, IT), np.uint32)
    w_rows[0:DENSE, IT - 1] = np.arange(DENSE)
    a0 = 0
    for m, n in enumerate(BLOCK_A):
        for a in range(n):
            for d in range(HALF):
                i, j = divmod((FIELDS + 1) * (a0 + a) + d + 1, FIELDS)
                w_rows[INNER_AT[m] + a * HALF + d, m] = triu[min(i, j), max(i, j)]
        a0 += n

    arrays = {
        "x_dense": np.ascontiguousarray(r_x_dense), "x_sparse": np.ascontiguousarray(r_x_sparse),
        "emb": np.ascontiguousarray(L0_rec_emb_tables), "w1": np.ascontiguousarray(L0_rec_w1),
        "b1": np.ascontiguousarray(L0_rec_b1), "w2": np.ascontiguousarray(L0_rec_w2),
        "b2": np.ascontiguousarray(L0_rec_b2), "w_rows": w_rows,
    }
    nc = bacc.Bacc("TRN2", target_bir_lowering=False, num_devices=1)
    args = [nc.dram_tensor(name, a.shape, mybir.dt.from_np(a.dtype), kind="ExternalInput").ap()
            for name, a in arrays.items()]
    out = nc.dram_tensor("out", (BATCH, 1), F32, kind="ExternalOutput").ap()
    gram_dram = nc.dram_tensor("gram_dram", (BT, ROWS_G, P), F32, kind="Internal").ap()
    build(nc, *args, out, gram_dram)
    return run_bass_kernel_spmd(nc, [arrays], core_ids=[0]).results[0]["out"]
```

```python
from contextlib import ExitStack

import concourse.bass as bass
from concourse import mybir

ALU = mybir.AluOpType
ACT = mybir.ActivationFunctionType
AX = mybir.AxisListType
F32 = mybir.dt.float32
F32R = mybir.dt.float32r
I32 = mybir.dt.int32
U32 = mybir.dt.uint32

P = 128
BATCH, DENSE, FIELDS, VOCAB, K = 512, 13, 26, 6250, 64
PAIRS = FIELDS * (FIELDS - 1) // 2
HID = DENSE + FIELDS * K + PAIRS
BT = BATCH // P

ZT = FIELDS // 2
ROWS_G = FIELDS * FIELDS
HALF = FIELDS // 2
BLOCK_A = [9, 9, 7]
INNER = [n * HALF for n in BLOCK_A]
IT = len(BLOCK_A)
NT = ZT + IT
INNER_AT = [0, 0, DENSE]
ONES_AT = DENSE + INNER[-1]
KROWS = [P] * ZT + INNER[:-1] + [ONES_AT + 1]

CHUNKS = [[(0, 502), (502, 500)], [(1002, 500), (1502, 500)]]
HALF_AT = [0, 1002]
HALF_W = [1002, 1000]
CHUNK_COLS = [[slice(at - HALF_AT[h], at - HALF_AT[h] + width) for at, width in CHUNKS[h]] for h in (0, 1)]
HW = max(HALF_W)

RAW = 5
HL = 5
GROUPS = P // 4
PER_BANK = 4
ROUNDS = GROUPS // PER_BANK
AUX = 6
LEAD = 3
WARM = 15
PACED = 16
FETCH = 14

PIECES = ([(0, t, h) for t in range(ZT) for h in (0, 1)]
          + [(0, t, h) for h in (1, 0) for t in range(ZT, NT)]
          + [(1, t, 1) for t in range(NT)] + [(2, t, 0) for t in range(NT)])
PIECE = {key: n for n, key in enumerate(PIECES)}
CELLS = {(0, 0): {0: 0, 1: 4}, (0, 1): {0: 2},
         (1, 1): {1: 0, 2: 2, 3: 4},
         (2, 0): {2: 0, 3: 2}}
RINGED = [n for n, (ph, t, h) in enumerate(PIECES) if t < ZT]
PLACED = [PIECE[0, t, 1] for t in range(ZT, NT)]


def products(ph, t):
    return [("product", PIECE[ph, t, h], bt) for h in ((0, 1) if ph == 0 else (2 - ph,)) for bt in CELLS[ph, h]]


def inner_products(ph, h, bt):
    return [("product", PIECE[ph, t, h], bt) for t in range(ZT, NT)]


def mixed(a, b):
    out = []
    for n in range(max(len(a), len(b))):
        out += a[n:n + 1] + b[n:n + 1]
    return out


def make_steps():
    def gram(bt):
        return [("gram", bt, rnd) for rnd in range(ROUNDS)]

    def first(t, h, bt):
        return ("product", PIECE[0, t, h], bt)

    todo = [("transpose", 0, 0), first(0, 0, 0), ("transpose", 0, 1), first(0, 1, 0), ("transpose", 1, 0)]
    for t in range(1, ZT - 1):
        todo += [first(t, 0, 0), ("transpose", 0, t + 1), first(t - 1, 0, 1), ("transpose", 1, t), first(t, 1, 0)]
    t = ZT - 1
    g, w = gram(0), [("split", n) for n in PLACED]
    todo += [first(t, 0, 0)] + g[:4] + [("transpose", 1, t), w[0], first(t - 1, 0, 1)] + g[4:] + [("bounce", 0)]
    g = gram(1)
    todo += [("constants",)] + g[:4] + [w[1], first(t, 1, 0)] + g[4:7] + [("inner", 0)] + g[7:] + [("bounce", 1)]
    todo += [w[2], first(t, 0, 1)]
    todo += inner_products(0, 1, 0)
    todo += mixed(inner_products(0, 0, 0) + inner_products(0, 0, 1),
                  [("transpose", bt, t) for t in range(3) for bt in (2, 3)])
    todo.insert(todo.index(("transpose", 2, 0)) + 1, ("inner", 1))
    for t in range(ZT - 3):
        p = products(1, t)
        todo += p[:1] + [("transpose", 2, t + 3)] + p[1:2] + [("transpose", 3, t + 3)] + p[2:]
    p = [s for t in range(ZT - 3, ZT) for s in products(1, t)]
    for bt in (2, 3):
        g = gram(bt)
        for n in range(0, ROUNDS, 2):
            todo += [p.pop(0)] + g[n:n + 2]
        todo += [("bounce", bt)]
    todo += p + [("inner", 2)] + inner_products(1, 1, 1) + inner_products(1, 1, 2)[:1] + [("inner", 3)]
    todo += inner_products(1, 1, 2)[1:] + inner_products(1, 1, 3)
    todo += [s for t in range(ZT) for s in products(2, t)] + inner_products(2, 0, 2) + inner_products(2, 0, 3)

    steps = []
    begun, split, loaded = -1, 0, 0
    left = [len(CELLS[ph, h]) for ph, t, h in PIECES]
    for step in todo:
        if step[0] == "product":
            begun = max(begun, step[1])
        due = step[0] != "transpose" or begun < 0
        ahead = begun + (LEAD if begun > 1 else 2)
        while due:
            if split in PLACED and ("split", split) in steps:
                split += 1
            elif (split <= min(ahead, len(PIECES) - 1) and split not in PLACED
                    and (split < HL or left[split - HL] == 0)
                    and (split not in RINGED or RINGED.index(split) < loaded)):
                steps.append(("split", split))
                split += 1
            elif (loaded < len(RINGED) and RINGED[loaded] <= begun + FETCH
                  and (loaded < RAW or RINGED[loaded - RAW] < split)):
                steps.append(("load", loaded))
                loaded += 1
            else:
                break
        steps.append(step)
        if step[0] == "product":
            left[step[1]] -= 1
    return steps


STEPS = make_steps()
PRODUCTS = [s[1:] for s in STEPS if s[0] == "product"]
TRANSPOSES = [s[1:] for s in STEPS if s[0] == "transpose"]
SPLITS = [s for s in STEPS if s[0] in ("transpose", "inner")]
GRAMS = [s[1:] for s in STEPS if s[0] == "gram"]
GATHERS = TRANSPOSES
W_IN_GATHERS = {2 * ZT - 2: (0,), 2 * ZT - 1: (1, 2)}
AUX_USES = [s for s in STEPS if s[0] in ("transpose", "gram")]
COMPLETE = {}
for _k, (_n, _bt) in enumerate(PRODUCTS):
    if PIECES[_n][1] == NT - 1:
        COMPLETE[_k] = (PIECES[_n][0], CELLS[PIECES[_n][0], PIECES[_n][2]][_bt])
DRAINS = list(COMPLETE.values())


def split_count(bt, t):
    return SPLITS.index(("transpose", bt, t) if t < ZT else ("inner", bt)) + 1


def transposed_count(bt, t):
    return TRANSPOSES.index((bt, t)) + 1


def et_count(bt, t):
    by_dve = [s for s in TRANSPOSES if s[0] == 1]
    by_act = [s for s in TRANSPOSES if s[0] != 1]
    return (by_dve if bt == 1 else by_act).index((bt, t)) + 1


def aux(step):
    return AUX + AUX_USES.index(step) % 2


def gram_count(bt, rnd):
    return GRAMS.index((bt, rnd)) + 1


def products_through(n):
    return max(k for k, p in enumerate(PRODUCTS) if p[0] == n) + 1


def build(nc, x_dense, x_sparse, emb, w1, b1, w2, b2, w_rows, out, gram_dram):
    with ExitStack() as ctx:
        def sb(name, shape, dt):
            return ctx.enter_context(nc.sbuf_tensor(name, shape, dt))

        def sem(name):
            return ctx.enter_context(nc.semaphore(name))

        x_idx = sb("x_idx", [P, BT, FIELDS], I32)
        field_base = sb("field_base", [P, BT, FIELDS], I32)
        wrap = sb("wrap", [P, BT, FIELDS], F32)
        wrapped = sb("wrapped", [P, BT, FIELDS], F32)
        row_idx = sb("row_idx", [P, BT, FIELDS], U32)
        w_row_idx = sb("w_row_idx", [P, IT], U32)
        dense = sb("dense", [P, BT, DENSE], F32)
        ones = sb("ones", [P, P], F32)
        ident = sb("ident", [P, P], F32)
        E = sb("E", [P, ZT, 2, 2, K], F32)
        ET = sb("ET", [P, GROUPS, 4, 32], F32)
        G = sb("G", [P, FIELDS, P], F32)
        x_in = sb("x_in", [P, BT, IT, P], F32)
        x_hi = sb("x_hi", [P, NT, BATCH], F32R)
        x_lo = sb("x_lo", [P, NT, BATCH], F32R)
        w_raw = sb("w_raw", [P, RAW, HW], F32)
        w_in = sb("w_in", [P, IT, HID], F32)
        w_hi = sb("w_hi", [P, HL, HW], F32R)
        w_lo = sb("w_lo", [P, HL, HW], F32R)
        w2_all = sb("w2_all", [P, HID], F32)
        b2_all = sb("b2_all", [P, 1], F32)
        parts = sb("parts", [P, BT, 4], F32)
        logit = sb("logit", [P, BT], F32)
        result = sb("result", [P, BT], F32)
        bank = [ctx.enter_context(nc.psum_tensor(f"bank{n}", [P, 512], F32)) for n in range(8)]

        idx_landed = sem("idx_landed")
        base_ready = sem("base_ready")
        idx_step = sem("idx_step")
        idx_ready = sem("idx_ready")
        w_row_idx_landed = sem("w_row_idx_landed")
        bias_landed = sem("bias_landed")
        consts_landed = sem("consts_landed")
        dense_landed = sem("dense_landed")
        ones_ready = sem("ones_ready")
        ident_ready = sem("ident_ready")
        et_pad_ready = sem("et_pad_ready")
        ones_row_ready = sem("ones_row_ready")
        w_in_landed = [sem(f"w_in_landed{m}") for m in range(IT)]
        e_landed = [[sem(f"e_landed{t}_{r}") for r in range(2)] for t in range(ZT)]
        w_landed = [sem(f"w_landed{n}") for n in range(RAW)]
        dense_transposed = sem("dense_transposed")
        dense_copied = sem("dense_copied")
        e_transposed = sem("e_transposed")
        et_ready_act = sem("et_ready_act")
        et_ready_dve = sem("et_ready_dve")
        x_hi_ready = sem("x_hi_ready")
        x_split = sem("x_split")
        w_hi_ready = sem("w_hi_ready")
        w_split = sem("w_split")
        products_done = sem("products_done")
        cell_done = sem("cell_done")
        drained = sem("drained")
        gram_done = sem("gram_done")
        g_copied_act = sem("g_copied_act")
        g_copied_dve = sem("g_copied_dve")
        g_stored = sem("g_stored")
        x_in_landed = [sem(f"x_in_landed{bt}") for bt in range(BT)]
        logit_ready = sem("logit_ready")
        result_ready = sem("result_ready")
        out_stored = sem("out_stored")

        emb_rows = emb.rearrange("f v k -> (f v) k")
        z_rows = w1[DENSE:DENSE + FIELDS * K, :].rearrange("(t p) n -> t p n", p=P)

        def w_source(n):
            ph, t, h = PIECES[n]
            if t < ZT:
                return w_raw[0:P, RINGED.index(n) % RAW, 0:HALF_W[h]]
            return w_in[0:KROWS[t], t - ZT, HALF_AT[h]:HALF_AT[h] + HALF_W[h]]

        def w_parts(n):
            ph, t, h = PIECES[n]
            return (w_hi[0:KROWS[t], n % HL, 0:HALF_W[h]], w_lo[0:KROWS[t], n % HL, 0:HALF_W[h]])

        def x_parts(bt, t):
            b = slice(bt * P, (bt + 1) * P)
            return x_hi[:, t, b], x_lo[:, t, b]

        INNER_PARTS = [(KROWS[ZT], slice(0, IT - 1)), (KROWS[NT - 1], slice(IT - 1, IT))]

        def x_inner_parts(bt, rows, tiles):
            b = slice(bt * P, (bt + 1) * P)
            return [x[0:rows, ZT + tiles.start:ZT + tiles.stop, b] for x in (x_hi, x_lo)]

        def et_view(src, f):
            return src[64 * f:64 * f + 64, 0:P].rearrange("k (s g) -> k s g", s=4)

        def et_place(r, t, f):
            return ET[64 * r:64 * r + 64, :, :, 2 * t + f].rearrange("k g s -> k s g")

        def gram_view(src, s):
            v = src[32 * s:32 * s + FIELDS, 0:PER_BANK * 4 * FIELDS]
            return v.rearrange("i (g s j) -> i g s j", g=PER_BANK, s=4)[:, :, s, :]

        def gram_place(r, s, rnd):
            v = G[32 * r:32 * r + FIELDS, :, 32 * s + PER_BANK * rnd:32 * s + PER_BANK * (rnd + 1)]
            return v.rearrange("i j g -> i g j")

        block = ctx.enter_context(nc.Block())

        @block.sync
        def _(sp):
            sp.dma_start(x_idx[:], x_sparse.rearrange("(p t) f -> p t f", t=BT)).then_inc(idx_landed, 16)
            for step in STEPS:
                if step[0] == "load":
                    m = step[1]
                    ph, t, h = PIECES[RINGED[m]]
                    if 3 <= m < PACED:
                        r, z = GATHERS[max(m - 4, 0)]
                        sp.wait_ge(e_landed[z][r], 32)
                    if m >= RAW:
                        sp.wait_ge(w_split, 2 * (RINGED[m - RAW] + 1))
                    sp.dma_start(w_source(RINGED[m]), z_rows[t, :, HALF_AT[h]:HALF_AT[h] + HALF_W[h]])\
                      .then_inc(w_landed[m % RAW], 16)
                    if m == 2 * RAW:
                        sp.dma_start(w_in[ONES_AT:ONES_AT + 1, IT - 1, :], b1.rearrange("(a n) -> a n", a=1))\
                          .then_inc(bias_landed, 16)
                if step[0] == "constants":
                    sp.dma_start(w2_all[:], w2.rearrange("n o -> (o n)").partition_broadcast(P))\
                      .then_inc(consts_landed, 16)
                    sp.dma_start(b2_all[:], b2.partition_broadcast(P)).then_inc(consts_landed, 16)
                if step[0] == "bounce":
                    bt = step[1]
                    r = bt % 2
                    sp.wait_ge(g_copied_act, gram_count(bt, ROUNDS - 1))
                    sp.wait_ge(g_copied_dve, gram_count(bt, ROUNDS - 1))
                    sp.dma_start(gram_dram[bt].rearrange("(i j) b -> i j b", i=FIELDS), G[32 * r:32 * r + FIELDS])\
                      .then_inc(g_stored, 16)
                    sp.wait_ge(g_stored, 16 * (bt + 1))
                    if bt == 0:
                        sp.wait_ge(ones_row_ready, 1)
                    a0 = 0
                    for m, n in enumerate(BLOCK_A):
                        flat = gram_dram[bt, (FIELDS + 1) * a0:(FIELDS + 1) * (a0 + n), :]
                        sp.dma_start(x_in[INNER_AT[m]:INNER_AT[m] + INNER[m], bt, m, :],
                                     flat.rearrange("(a d) b -> a d b", a=n)[:, 1:1 + HALF, :])\
                          .then_inc(x_in_landed[bt], 16)
                        a0 += n
            sp.wait_ge(result_ready, 1)
            sp.dma_start(out.rearrange("(p t) o -> p (t o)", t=BT), result[:]).then_inc(out_stored, 16)
            sp.wait_ge(out_stored, 16)

        @block.gpsimd
        def _(pool):
            nc.gpsimd.iota(field_base[:], [[0, BT], [VOCAB, FIELDS]], base=0, channel_multiplier=0)\
              .then_inc(base_ready, 1)
            nc.gpsimd.memset(ones[:], 1.0).then_inc(ones_ready, 1)
            nc.gpsimd.memset(ET[:, :, :, FIELDS:32], 0.0).then_inc(et_pad_ready, 1)
            pool.wait_ge(ones_ready, 1)
            nc.gpsimd.affine_select(out=ident[:], in_=ones[:], compare_op=ALU.is_equal, fill=0.0, base=0,
                                    pattern=[[-1, P]], channel_multiplier=1).then_inc(ident_ready, 1)
            pool.wait_ge(idx_ready, 1)
            for k, (bt, t) in enumerate(GATHERS):
                if bt >= 2:
                    pool.wait_ge(e_transposed, transposed_count(bt - 2, t))
                for f in range(2):
                    at = row_idx[:, bt, 2 * t + f:2 * t + f + 1]
                    nc.gpsimd.indirect_dma_start(
                        out=E[:, t, bt % 2, f, :], out_offset=None, in_=emb_rows,
                        in_offset=bass.IndirectOffsetOnAxis(ap=at, axis=0)).then_inc(e_landed[t][bt % 2], 16)
                for m in W_IN_GATHERS.get(k, ()):
                    n = INNER_AT[m] + INNER[m]
                    pool.wait_ge(w_row_idx_landed, 16)
                    nc.gpsimd.indirect_dma_start(
                        out=w_in[0:n, m, :], out_offset=None, in_=w1,
                        in_offset=bass.IndirectOffsetOnAxis(ap=w_row_idx[0:n, m:m + 1], axis=0))\
                      .then_inc(w_in_landed[m], 16)

        @block.scalar
        def _(act):
            act.dma_start(dense[:], x_dense.rearrange("(p t) d -> p t d", t=BT))\
               .then_inc(dense_landed, 16)
            act.dma_start(w_row_idx[:], w_rows).then_inc(w_row_idx_landed, 16)
            act.wait_ge(dense_transposed, 1)
            nc.scalar.copy(x_in[0:DENSE, :, IT - 1, :],
                           bank[AUX][0:DENSE, :].rearrange("p (a b) -> p a b", a=BT)).then_inc(dense_copied, 1)
            for step in STEPS:
                if step[0] == "split":
                    n = step[1]
                    if PIECES[n][1] < ZT:
                        m = RINGED.index(n)
                        act.wait_ge(w_landed[m % RAW], 16 * (m // RAW + 1))
                    else:
                        act.wait_ge(w_in_landed[PIECES[n][1] - ZT], 16)
                        if PIECES[n][1] == NT - 1:
                            act.wait_ge(bias_landed, 16)
                    if n >= HL:
                        act.wait_ge(products_done, products_through(n - HL))
                    for cols in CHUNK_COLS[PIECES[n][2]]:
                        nc.scalar.copy(w_parts(n)[0][:, cols], w_source(n)[:, cols]).then_inc(w_hi_ready, 1)
                if step[0] == "transpose":
                    bt, t = step[1:]
                    src = bank[aux(step)]
                    act.wait_ge(e_transposed, transposed_count(bt, t))
                    nc.scalar.copy(x_parts(bt, t)[0], src[:, 0:P]).then_inc(x_hi_ready, 1)
                    if bt != 1:
                        if bt >= 2:
                            act.wait_ge(gram_done, gram_count(bt - 2, ROUNDS - 1))
                        for f in range(2):
                            last = nc.scalar.copy(et_place(bt % 2, t, f), et_view(src, f))
                        last.then_inc(et_ready_act, 1)
                if step[0] == "gram":
                    bt, rnd = step[1:]
                    act.wait_ge(gram_done, gram_count(bt, rnd))
                    if bt >= 2:
                        act.wait_ge(g_stored, 16 * (bt - 1))
                    for s in (0, 1):
                        last = nc.scalar.copy(gram_place(bt % 2, s, rnd), gram_view(bank[aux(step)], s))
                    last.then_inc(g_copied_act, 1)
                if step[0] == "inner":
                    bt = step[1]
                    act.wait_ge(x_in_landed[bt], 16 * IT)
                    if bt == 0:
                        act.wait_ge(dense_copied, 1)
                        act.wait_ge(ones_row_ready, 1)
                    for rows, tiles in INNER_PARTS:
                        last = nc.scalar.copy(x_inner_parts(bt, rows, tiles)[0], x_in[0:rows, bt, tiles, :])
                    last.then_inc(x_hi_ready, 1)
            act.wait_ge(logit_ready, 1)
            act.wait_ge(consts_landed, 32)
            nc.scalar.activation(result[:], logit[:], ACT.Sigmoid, bias=b2_all[:, 0:1]).then_inc(result_ready, 1)

        @block.vector
        def _(dve):
            dve.wait_ge(idx_landed, 16)
            nc.vector.tensor_scalar(wrap[:], x_idx[:], 0.0, float(VOCAB), ALU.is_lt, ALU.mult).then_inc(idx_step, 1)
            dve.wait_ge(idx_step, 1)
            nc.vector.scalar_tensor_tensor(out=wrapped[:], in0=x_idx[:], scalar=float(VOCAB - 1), in1=wrap[:],
                                           op0=ALU.min, op1=ALU.add).then_inc(idx_step, 1)
            dve.wait_ge(idx_step, 2)
            dve.wait_ge(base_ready, 1)
            nc.vector.scalar_tensor_tensor(out=row_idx[:], in0=wrapped[:], scalar=0.0, in1=field_base[:],
                                           op0=ALU.max, op1=ALU.add).then_inc(idx_ready, 1)
            nc.vector.memset(x_in[96:ONES_AT + 1, :, IT - 1, :], 1.0).then_inc(ones_row_ready, 1)

            for step in STEPS:
                if step[0] == "split":
                    n = step[1]
                    for q, cols in enumerate(CHUNK_COLS[PIECES[n][2]]):
                        dve.wait_ge(w_hi_ready, 2 * n + q + 1)
                        hi, lo = [w[:, cols] for w in w_parts(n)]
                        nc.vector.tensor_tensor(lo, w_source(n)[:, cols], hi.bitcast(F32), ALU.subtract)\
                          .then_inc(w_split, 1)
                if step[0] == "transpose":
                    bt, t = step[1:]
                    src = bank[aux(step)]
                    dve.wait_ge(x_hi_ready, SPLITS.index(step) + 1)
                    if bt != 1:
                        dve.wait_ge(et_ready_act, et_count(bt, t))
                    hi, lo = x_parts(bt, t)
                    nc.vector.tensor_tensor(lo, src[:, 0:P], hi.bitcast(F32), ALU.subtract).then_inc(x_split, 1)
                    if bt == 1:
                        for f in range(2):
                            last = nc.vector.tensor_copy(et_place(1, t, f), et_view(src, f))
                        last.then_inc(et_ready_dve, 1)
                if step[0] == "gram":
                    bt, rnd = step[1:]
                    dve.wait_ge(gram_done, gram_count(bt, rnd))
                    if bt >= 2:
                        dve.wait_ge(g_stored, 16 * (bt - 1))
                    for s in (2, 3):
                        last = nc.vector.tensor_copy(gram_place(bt % 2, s, rnd), gram_view(bank[aux(step)], s))
                    last.then_inc(g_copied_dve, 1)
                if step[0] == "inner":
                    bt = step[1]
                    dve.wait_ge(x_hi_ready, SPLITS.index(step) + 1)
                    for rows, tiles in INNER_PARTS:
                        hi, lo = x_inner_parts(bt, rows, tiles)
                        last = nc.vector.tensor_tensor(lo, x_in[0:rows, bt, tiles, :], hi.bitcast(F32), ALU.subtract)
                    last.then_inc(x_split, 1)
                if step[0] == "product" and PIECES[step[1]][1] == NT - 1:
                    n, bt = step[1:]
                    ph, t, h = PIECES[n]
                    if (ph, CELLS[ph, h][bt]) == DRAINS[0]:
                        dve.wait_ge(consts_landed, 32)
                    for q, (at, width) in enumerate(CHUNKS[h]):
                        if q == 0:
                            dve.wait_ge(cell_done, DRAINS.index((ph, CELLS[ph, h][bt])) + 1)
                        else:
                            dve.wait_ge(products_done, PRODUCTS.index((n, bt)) + 1)
                        cell = bank[CELLS[ph, h][bt] + q][:, 0:width]
                        nc.vector.scalar_tensor_tensor(
                            out=cell, in0=cell, scalar=0.0, in1=w2_all[:, at:at + width], op0=ALU.max,
                            op1=ALU.mult, accum_out=parts[:, bt, 2 * h + q:2 * h + q + 1]).then_inc(drained, 1)
            dve.wait_ge(drained, 2 * len(DRAINS))
            nc.vector.tensor_reduce(logit[:], parts[:], AX.X, ALU.add).then_inc(logit_ready, 1)

        @block.tensor
        def _(pe):
            pe.wait_ge(ident_ready, 1)
            pe.wait_ge(dense_landed, 16)
            for bt in range(BT):
                last = nc.tensor.transpose(bank[AUX][0:DENSE, bt * P:(bt + 1) * P], dense[:, bt, :], ident[:])
            last.then_inc(dense_transposed, 1)
            for n in range(WARM):
                nc.tensor.matmul(bank[0][:, 0:P], ident[:], ones[:], start=True, stop=True)

            def wait_aux(step):
                n = AUX_USES.index(step) - 2
                if n == -2:
                    pe.wait_ge(dense_copied, 1)
                if n < 0:
                    return
                kind, bt, k = AUX_USES[n]
                if kind == "gram":
                    pe.wait_ge(g_copied_act, gram_count(bt, k))
                    pe.wait_ge(g_copied_dve, gram_count(bt, k))
                elif bt == 1:
                    pe.wait_ge(et_ready_dve, et_count(bt, k))
                else:
                    pe.wait_ge(x_split, split_count(bt, k))

            for step in STEPS:
                if step[0] == "transpose":
                    bt, t = step[1:]
                    pe.wait_ge(e_landed[t][bt % 2], 32 * (bt // 2 + 1))
                    wait_aux(step)
                    nc.tensor.transpose(bank[aux(step)][:, 0:P], E[:, t, bt % 2, :, :].rearrange("p f k -> p (f k)"),
                                        ident[:]).then_inc(e_transposed, 1)
                if step[0] == "gram":
                    bt, rnd = step[1:]
                    r = bt % 2
                    wait_aux(step)
                    if rnd == 0:
                        pe.wait_ge(et_ready_dve if bt == 1 else et_ready_act, et_count(bt, ZT - 1))
                        if bt == 0:
                            pe.wait_ge(et_pad_ready, 1)
                    for q in range(PER_BANK):
                        e = ET[64 * r:64 * r + 64, PER_BANK * rnd + q]
                        last = nc.tensor.matmul(
                            bank[aux(step)][:, q * 4 * FIELDS:(q + 1) * 4 * FIELDS],
                            e.rearrange("k s f -> k (s f)"), e[:, :, 0:FIELDS], start=True, stop=True)
                    last.then_inc(gram_done, 1)
                if step[0] == "product":
                    n, bt = step[1:]
                    ph, t, h = PIECES[n]
                    b0 = CELLS[ph, h][bt]
                    pe.wait_ge(w_split, 2 * (n + 1))
                    pe.wait_ge(x_split, split_count(bt, t))
                    if t == 0 and ph > 0:
                        pe.wait_ge(drained, 2 * (DRAINS.index((ph - 1, b0)) + 1))
                    hi, lo = w_parts(n)
                    xh = x_hi[0:KROWS[t], t, bt * P:(bt + 1) * P]
                    xl = x_lo[0:KROWS[t], t, bt * P:(bt + 1) * P]
                    for q, cols in enumerate(CHUNK_COLS[h]):
                        for m, (x, w) in enumerate(((xh, hi), (xh, lo), (xl, hi))):
                            last = nc.tensor.matmul(bank[b0 + q][:, 0:CHUNKS[h][q][1]], x, w[:, cols],
                                                    start=(t == 0 and m == 0), stop=(t == NT - 1 and m == 2))
                        if q == 0 and t == NT - 1:
                            last.then_inc(cell_done, 1)
                    last.then_inc(products_done, 1)


def kernel(r_x_dense, r_x_sparse, L0_rec_emb_tables, L0_rec_w1, L0_rec_b1, L0_rec_w2, L0_rec_b2):
    import numpy as np
    import concourse.bacc as bacc
    from concourse.bass_utils import run_bass_kernel_spmd

    triu = {}
    for i in range(FIELDS):
        for j in range(i + 1, FIELDS):
            triu[i, j] = DENSE + FIELDS * K + len(triu)
    w_rows = np.zeros((P, IT), np.uint32)
    w_rows[0:DENSE, IT - 1] = np.arange(DENSE)
    a0 = 0
    for m, n in enumerate(BLOCK_A):
        for a in range(n):
            for d in range(HALF):
                i, j = divmod((FIELDS + 1) * (a0 + a) + d + 1, FIELDS)
                w_rows[INNER_AT[m] + a * HALF + d, m] = triu[min(i, j), max(i, j)]
        a0 += n

    arrays = {
        "x_dense": np.ascontiguousarray(r_x_dense), "x_sparse": np.ascontiguousarray(r_x_sparse),
        "emb": np.ascontiguousarray(L0_rec_emb_tables), "w1": np.ascontiguousarray(L0_rec_w1),
        "b1": np.ascontiguousarray(L0_rec_b1), "w2": np.ascontiguousarray(L0_rec_w2),
        "b2": np.ascontiguousarray(L0_rec_b2), "w_rows": w_rows,
    }
    nc = bacc.Bacc("TRN2", target_bir_lowering=False, num_devices=1)
    args = [nc.dram_tensor(name, a.shape, mybir.dt.from_np(a.dtype), kind="ExternalInput").ap()
            for name, a in arrays.items()]
    out = nc.dram_tensor("out", (BATCH, 1), F32, kind="ExternalOutput").ap()
    gram_dram = nc.dram_tensor("gram_dram", (BT, ROWS_G, P), F32, kind="Internal").ap()
    build(nc, *args, out, gram_dram)
    return run_bass_kernel_spmd(nc, [arrays], core_ids=[0]).results[0]["out"]
```
